# Optimizing a Trainium2 kernel written in Bass

```python
import numpy as np
import jax
import jax.numpy as jnp

def _softmax(x, axis=-1):
    return jax.nn.softmax(x, axis=axis)

def _gelu(x):
    return jax.nn.gelu(x, approximate=True)

def _silu(x):
    return jax.nn.silu(x)

def _sigmoid(x):
    return jax.nn.sigmoid(x)

def _layernorm(x, axis=-1, eps=1e-05):
    m = jnp.mean(x, axis=axis, keepdims=True)
    v = jnp.var(x, axis=axis, keepdims=True)
    return (x - m) / jnp.sqrt(v + eps)

def _scatter_add(tgt, idx, src, axis=0):
    return tgt.at[idx].add(src)

def _segment_sum(src, seg, n):
    return jax.ops.segment_sum(src, seg, n)
kernel_name = 'mk_gnn_resnorm_d2_gnn_r32_cca4fb'

def setup_inputs(seed: int=0):
    np.random.seed(seed)
    _w = jnp.asarray

    def _rec_inputs():
        import jax
        import jax.numpy as jnp
        _gk = jax.random.key(seed)
        x = -0.0003713 + 1 * jax.random.normal(jax.random.fold_in(_gk, 1), (3125, 128), jnp.float32)
        src = jax.random.randint(jax.random.fold_in(_gk, 2), (50000,), 0, 3125, jnp.int32)
        dst = jnp.minimum((3125 * jax.random.uniform(jax.random.fold_in(_gk, 3), (50000,)) ** 2.0).astype(jnp.int32), 99999)
        _o = jnp.argsort(dst, stable=True)
        src = src[_o]
        dst = dst[_o]
        edge_type_65 = jax.random.randint(jax.random.fold_in(_gk, 12), (50000,), 0, 65, jnp.int32)
        return (x, src, dst, edge_type_65)
    x, src, dst, edge_type_65 = _rec_inputs()

    def _L0_gnn_setup():
        import jax, jax.numpy as jnp
        import numpy as np
        BN_EPS = 1e-05
        key = jax.random.key(seed)
        ks = jax.random.split(key, 8)
        N, E, D, H = (3125, 50000, 128, 128)
        x = jax.random.normal(ks[0], (N, D), dtype=jnp.float32)
        edge_index = jax.random.randint(ks[1], (2, E), 0, N, dtype=jnp.int64)
        s1 = 1.0 / np.sqrt(D)
        s2 = 1.0 / np.sqrt(H)
        w1 = jax.random.uniform(ks[2], (D, H), jnp.float32, -s1, s1)
        b1 = jax.random.uniform(ks[3], (H,), jnp.float32, -s1, s1)
        w2 = jax.random.uniform(ks[4], (H, H), jnp.float32, -s2, s2)
        b2 = jax.random.uniform(ks[5], (H,), jnp.float32, -s2, s2)
        gamma = jnp.ones((H,), jnp.float32)
        beta = jnp.zeros((H,), jnp.float32)
        return {'x': x, 'edge_index': edge_index, 'w1': w1, 'b1': b1, 'w2': w2, 'b2': b2, 'gamma': gamma, 'beta': beta}
    _L0_gnn_all = _L0_gnn_setup()
    _L0_gnn_in = {k: v for k, v in _L0_gnn_all.items() if k in ('w1', 'b1', 'w2', 'b2', 'gamma', 'beta')}
    del _L0_gnn_all

    def _L1_gnn_setup():
        import jax, jax.numpy as jnp
        import numpy as np
        EPS = 1e-05
        key = jax.random.key(seed)
        ks = jax.random.split(key, 10)
        N, E, F_IN, F_OUT, R = (625, 20000, 128, 128, 65)
        x = jax.random.normal(ks[0], (N, F_IN), dtype=jnp.float32)
        edge_index = jax.random.randint(ks[1], (2, E), 0, N, dtype=jnp.int64)
        edge_type = jax.random.randint(ks[2], (E,), 0, R, dtype=jnp.int64)
        s = 1.0 / np.sqrt(F_IN)
        W_rel = jax.random.normal(ks[3], (R, F_IN, F_OUT), dtype=jnp.float32) * s
        W_root = jax.random.normal(ks[4], (F_IN, F_OUT), dtype=jnp.float32) * s
        bias = jax.random.normal(ks[5], (F_OUT,), dtype=jnp.float32) * s
        W_res = jax.random.normal(ks[6], (F_IN, F_OUT), dtype=jnp.float32) * s
        b_res = jax.random.normal(ks[7], (F_OUT,), dtype=jnp.float32) * s
        gamma = jnp.ones((F_OUT,), dtype=jnp.float32)
        beta = jnp.zeros((F_OUT,), dtype=jnp.float32)
        return {'x': x, 'edge_index': edge_index, 'edge_type': edge_type, 'W_rel': W_rel, 'W_root': W_root, 'bias': bias, 'W_res': W_res, 'b_res': b_res, 'gamma': gamma, 'beta': beta}
    _L1_gnn_all = _L1_gnn_setup()
    _L1_gnn_in = {k: v for k, v in _L1_gnn_all.items() if k in ('W_rel', 'W_root', 'bias', 'W_res', 'b_res', 'gamma', 'beta')}
    del _L1_gnn_all
    return {'x': x, 'src': src, 'dst': dst, 'edge_type_65': edge_type_65, 'L0_gnn_w1': _L0_gnn_in['w1'], 'L0_gnn_b1': _L0_gnn_in['b1'], 'L0_gnn_w2': _L0_gnn_in['w2'], 'L0_gnn_b2': _L0_gnn_in['b2'], 'L0_gnn_gamma': _L0_gnn_in['gamma'], 'L0_gnn_beta': _L0_gnn_in['beta'], 'L1_gnn_W_rel': _L1_gnn_in['W_rel'], 'L1_gnn_W_root': _L1_gnn_in['W_root'], 'L1_gnn_bias': _L1_gnn_in['bias'], 'L1_gnn_W_res': _L1_gnn_in['W_res'], 'L1_gnn_b_res': _L1_gnn_in['b_res'], 'L1_gnn_gamma': _L1_gnn_in['gamma'], 'L1_gnn_beta': _L1_gnn_in['beta']}

def reference(x, src, dst, edge_type_65, L0_gnn_w1, L0_gnn_b1, L0_gnn_w2, L0_gnn_b2, L0_gnn_gamma, L0_gnn_beta, L1_gnn_W_rel, L1_gnn_W_root, L1_gnn_bias, L1_gnn_W_res, L1_gnn_b_res, L1_gnn_gamma, L1_gnn_beta):
    import jax
    import jax.numpy as jnp

    def _L0_gnn_ref(x, edge_index, w1, b1, w2, b2, gamma, beta):
        import jax, jax.numpy as jnp
        import numpy as np
        BN_EPS = 1e-05
        N = x.shape[0]
        src, dst = (edge_index[0], edge_index[1])
        agg = jax.ops.segment_sum(x[src], dst, num_segments=N)
        h = x + agg
        h = jax.nn.relu(h @ w1 + b1) @ w2 + b2
        h = jax.nn.relu(h)
        mean = jnp.mean(h, axis=0)
        var = jnp.var(h, axis=0)
        return (h - mean) * jax.lax.rsqrt(var + BN_EPS) * gamma + beta

    def _L1_gnn_ref(x, edge_index, edge_type, W_rel, W_root, bias, W_res, b_res, gamma, beta):
        import jax, jax.numpy as jnp
        import numpy as np
        EPS = 1e-05
        N, F_in = x.shape
        R = W_rel.shape[0]
        src, dst = (edge_index[0], edge_index[1])
        seg = dst * R + edge_type
        msrc = x[src]
        sums = jax.ops.segment_sum(msrc, seg, num_segments=N * R).reshape(N, R, F_in)
        cnt = jax.ops.segment_sum(jnp.ones_like(seg, dtype=x.dtype), seg, num_segments=N * R).reshape(N, R, 1)
        agg = sums / jnp.maximum(cnt, 1.0)
        conv = jnp.einsum('nri,rio->no', agg, W_rel) + x @ W_root + bias
        h = conv + x @ W_res + b_res
        mean = h.mean(axis=0)
        var = jnp.mean(jnp.square(h - mean), axis=0)
        h = (h - mean) * jax.lax.rsqrt(var + EPS) * gamma + beta
        return jax.nn.relu(h)
    edge_index = jnp.stack([src, dst])
    x = _layernorm(x + _L0_gnn_ref(x, edge_index, L0_gnn_w1, L0_gnn_b1, L0_gnn_w2, L0_gnn_b2, L0_gnn_gamma, L0_gnn_beta), axis=-1)
    x = _layernorm(x + _L1_gnn_ref(x, edge_index, edge_type_65, L1_gnn_W_rel, L1_gnn_W_root, L1_gnn_bias, L1_gnn_W_res, L1_gnn_b_res, L1_gnn_gamma, L1_gnn_beta), axis=-1)
    return x

_drawn_inputs = setup_inputs


def setup_inputs(seed=0):
    import zlib

    import numpy as np

    out = dict(_drawn_inputs(seed))
    spreads = {'L0_gnn_gamma': (1.0, 0.2),
     'L0_gnn_beta': (0.0, 0.1),
     'L1_gnn_gamma': (1.0, 0.2),
     'L1_gnn_beta': (0.0, 0.1)}
    factors = {'L0_gnn_b1': 2.797, 'L1_gnn_bias': 8.0, 'L1_gnn_b_res': 8.0}
    for name, (base, spread) in spreads.items():
        noise = np.random.default_rng([zlib.crc32(name.encode()), seed]).standard_normal(out[name].shape)
        drawn = base * np.exp(spread * noise) if base else spread * noise
        out[name] = jnp.asarray(drawn.astype(out[name].dtype))
    for name, factor in factors.items():
        out[name] = (out[name] * factor).astype(out[name].dtype)
    return out
```

```python
import concourse.bass as bass
from concourse import mybir
from contextlib import ExitStack


def gnn_gin_then_relational_kernel(
    nc: bass.Bass,
    x: bass.AP,
    src: bass.AP,
    dst: bass.AP,
    edge_type: bass.AP,
    w1: bass.AP,
    b1: bass.AP,
    w2: bass.AP,
    b2: bass.AP,
    gamma0: bass.AP,
    beta0: bass.AP,
    w_rel: bass.AP,
    w_root: bass.AP,
    bias: bass.AP,
    w_res: bass.AP,
    b_res: bass.AP,
    gamma1: bass.AP,
    beta1: bass.AP,
    out: bass.AP,
):
    f32 = mybir.dt.float32
    bf16 = mybir.dt.bfloat16
    i32 = mybir.dt.int32
    ALU = mybir.AluOpType
    ACT = mybir.ActivationFunctionType
    AX = mybir.AxisListType
    ds = bass.ds

    P = 128
    N, D = x.shape
    E = src.shape[0]
    R = w_rel.shape[0]
    EPS = 1e-5

    BLOCKS = -(-N // P)
    NPAD = BLOCKS * P
    TAIL = N - (BLOCKS - 1) * P
    CHUNKS = -(-E // P)
    GROUP = 4
    RING = 32
    HALF = RING // 2
    GROUPS = RING // GROUP
    ITERS = -(-(CHUNKS + BLOCKS - 1) // RING)
    SLOTS = ITERS * RING
    SCOLS = -(-SLOTS // P)
    SLAST = SLOTS - (SCOLS - 1) * P
    BUCKETS = BLOCKS + 1
    PAD_DST = BLOCKS * P
    ECOLS = CHUNKS
    EFULL = (E // ECOLS) * ECOLS
    EREST = E - EFULL
    EP = E // ECOLS
    CREST = E - (CHUNKS - 1) * P
    BANK = 512
    NBANKS = -(-NPAD // BANK)
    CW = [(c * BANK, min(BANK, N - c * BANK)) for c in range(NBANKS)]
    TPB = BANK // P

    RO = R * D
    YW = 416
    YPAIRS = RO // (2 * YW)
    BPAIRS = 4
    YHALF = RO // 2
    HPAIR = YPAIRS // 2
    assert YPAIRS * 2 * YW == RO and (2 * YPAIRS) % BPAIRS == 0 and YPAIRS % 2 == 0
    YLOOPS = (BLOCKS - 1) // 2

    edges = nc.dram_tensor("edges", (CHUNKS, 3 * P), i32, kind="Internal").ap()
    slot_types = nc.dram_tensor("slot_types", (SLOTS, P), bf16, kind="Internal").ap()
    table = nc.dram_tensor("table", (N, RO), f32, kind="Internal").ap()
    table_rows = table.rearrange("n (r o) -> (n r) o", o=D)
    edges3 = edges.rearrange("c (k e) -> c k e", k=3)
    edges_flat = edges.rearrange("c (k o) -> (c k) o", o=1)

    ctx = ExitStack()
    with ctx:
        def sb(name, shape, dt):
            return ctx.enter_context(nc.sbuf_tensor(name, shape, dt))

        def sem(name):
            return ctx.enter_context(nc.semaphore(name))

        iota_i = sb("iota_i", [P, P], i32)
        part_i = sb("part_i", [P, SCOLS], i32)
        iota_row = sb("iota_row", [P, P], f32)
        slot_no = sb("slot_no", [P, SCOLS], f32)
        ident = sb("ident", [P, P], f32)
        before = sb("before", [P, P], f32)
        ones = sb("ones", [P, P], f32)
        avg = sb("avg", [P, P], f32)
        w1_sb = sb("w1_sb", [P, D], f32)
        w2_sb = sb("w2_sb", [P, D], f32)
        wroot_sb = sb("wroot_sb", [P, D], f32)
        wres_sb = sb("wres_sb", [P, D], f32)
        wrel_sb = sb("wrel_sb", [P, R, D], f32)
        vec = sb("vec", [P, 8], f32)
        V_B1, V_B2, V_G0, V_E0, V_BIAS, V_BRES, V_G1, V_E1 = range(8)
        bias_sum = sb("bias_sum", [P, 1], f32)
        eps_sb = sb("eps_sb", [P, 1], f32)

        counts = sb("counts", [P, BUCKETS + 1], f32)
        tot = sb("tot", [P, BUCKETS + 1], f32)
        zeros = sb("zeros", [P, BUCKETS], f32)
        ends = sb("ends", [P, BUCKETS], f32)
        starts = sb("starts", [P, BUCKETS], f32)
        ends_i = sb("ends_i", [P, BUCKETS], i32)
        starts_i = sb("starts_i", [P, BUCKETS], i32)
        span = sb("span", [P, BUCKETS], f32)
        nslots = sb("nslots", [P, BUCKETS], f32)
        slot_end = sb("slot_end", [P, BUCKETS], f32)
        shift = sb("shift", [P, BUCKETS], f32)
        cmp = sb("cmp", [P, SCOLS, BUCKETS], f32)
        pick = sb("pick", [P, SCOLS, BUCKETS], f32)
        slot_block = sb("slot_block", [P, SCOLS], f32)
        slot_shift = sb("slot_shift", [P, SCOLS], f32)
        slot_chunk = sb("slot_chunk", [P, SCOLS], f32)
        slot_chunk_i = sb("slot_chunk_i", [P, SCOLS], i32)
        block_base = sb("block_base", [P, SCOLS], f32)
        block_col = sb("block_col", [P, SCOLS], f32)
        offs = sb("offs", [1, SCOLS * P], i32)
        flag = sb("flag", [1, 1], i32)
        pad_edges = sb("pad_edges", [1, 3, P - CREST], i32)
        type_rows = sb("type_rows", [P, SCOLS, P], bf16)
        src_t = sb("src_t", [P, SLOTS], i32)
        key_t = sb("key_t", [P, SLOTS], i32)
        dloc_t = sb("dloc_t", [P, SLOTS + GROUP], f32)
        type_t = sb("type_t", [P, SLOTS + GROUP], f32)

        xT = sb("xT", [P, NPAD], f32)
        x1T = sb("x1T", [P, NPAD], f32)
        rel_count = sb("rel_count", [R, NPAD], f32)

        idx_now = sb("idx_now", [P, RING], i32)
        rows = sb("rows", [P, RING, D], f32)
        onehot = sb("onehot", [P, 2, GROUP, P], f32)
        onetype = sb("onetype", [P, 2, GROUP, R], f32)
        type_bc = sb("type_bc", [R, 2, HALF * P], bf16)
        type_oh = sb("type_oh", [R, 2, GROUP * P], f32)
        x1_tile = sb("x1_tile", [P, 2, P], f32)

        stage = sb("stage", [P, 2, RO], f32)
        flat = stage[:, :, :].rearrange("p a b -> p (a b)")
        hT = flat[:, 0:NPAD]
        gT = flat[:, NPAD:2 * NPAD]
        sqT = flat[:, 2 * NPAD:3 * NPAD]
        x_in = flat[:, 3 * NPAD:4 * NPAD].rearrange("p (t f) -> p t f", f=P)
        y_out = x_in
        base = 4 * NPAD
        slot_rows = flat[:, base:base + SCOLS * 3 * P].bitcast(i32).rearrange("p (j k e) -> p j k e", j=SCOLS, k=3)
        base += SCOLS * 3 * P
        slot_vals = flat[:, base:base + 4 * SCOLS * P].rearrange("p (k j e) -> p k j e", k=4, j=SCOLS)
        K_SRC, K_DLOC, K_TYPE, K_KEY = range(4)

        def prep(n):
            a = 2 * NPAD + n * ECOLS
            return flat[:, a:a + ECOLS]

        edge_data = flat[:, 2 * NPAD:2 * NPAD + 3 * ECOLS].bitcast(i32).rearrange("p (k e) -> p k e", k=3)
        dst_i = edge_data[:, 1, :]
        dst_next = prep(3).bitcast(i32)
        block_i = prep(4).bitcast(i32)
        block_f = prep(5)
        mask = prep(6)
        lane = prep(7)
        rank = flat[:, 0:ECOLS]
        pos = flat[:, ECOLS:2 * ECOLS]
        zrow = flat[:, 2 * ECOLS:3 * ECOLS]
        pos_i = flat[:, 3 * ECOLS:4 * ECOLS].bitcast(i32)
        hi_i = flat[:, 4 * ECOLS:5 * ECOLS].bitcast(i32)
        hi_f = flat[:, 5 * ECOLS:6 * ECOLS]
        addr_i = flat[:, 6 * ECOLS:9 * ECOLS].bitcast(i32).rearrange("p (k e) -> p k e", k=3)
        bucket_off = sb("bucket_off", [P, BUCKETS], f32)
        scat_idx = sb("scat_idx", [P, 3], i32)
        scat_val = sb("scat_val", [P, 3], i32)

        bn6 = sb("bn6", [P, NBANKS, 6], f32)
        bn2 = sb("bn2", [P, 2], f32)
        bn_sd = sb("bn_sd", [P, 1], f32)
        bn_rs = sb("bn_rs", [P, 1], f32)
        bn_scale = sb("bn_scale", [P, 1], f32)
        bn_ms = sb("bn_ms", [P, 1], f32)
        bn_shift = sb("bn_shift", [P, 1], f32)

        ps = ctx.enter_context(nc.psum_tensor("ps", [P, 8 * BANK], f32))
        acc = ps[:, 0:NBANKS * BANK]
        aux = ps[:, 7 * BANK:8 * BANK]

        def bank(c, w=BANK):
            return ps[:, c * BANK:c * BANK + w]

        def bank_pair(n):
            return ps[:, 2 * BANK * n:2 * BANK * (n + 1)].rearrange("p (b c) -> p b c", b=2)[:, :, 0:YW]

        s_iota = sem("s_iota")
        s_const = sem("s_const")
        s_dst0 = sem("s_dst0")
        s_dst = sem("s_dst")
        s_pad = sem("s_pad")
        s_edges = sem("s_edges")
        s_x = sem("s_x")
        s_w = sem("s_w")
        s_wrel = sem("s_wrel")
        s_cnt = sem("s_cnt")
        s_tot = sem("s_tot")
        s_flag = sem("s_flag")
        s_chunk = sem("s_chunk")
        s_bcol = sem("s_bcol")
        s_offp = sem("s_offp")
        s_off = sem("s_off")
        s_srows = sem("s_srows")
        s_vals = sem("s_vals")
        s_trows = sem("s_trows")
        s_tdram = sem("s_tdram")
        s_valt = sem("s_valt")
        s_tables = sem("s_tables")
        s_xtp = sem("s_xtp")
        s_xt = sem("s_xt")
        s_pos = sem("s_pos")
        s_sdata0 = sem("s_sdata0")
        s_sdata = sem("s_sdata")
        s_scopy = sem("s_scopy")
        s_scat = sem("s_scat")
        s_idx = sem("s_idx")
        s_row = [sem(f"s_row{j}") for j in range(RING)]
        s_slot = sem("s_slot")
        s_onehot = sem("s_onehot")
        s_cmm = sem("s_cmm")
        s_cadd = sem("s_cadd")
        s_h = sem("s_h")
        s_m1 = sem("s_m1")
        s_h1 = sem("s_h1")
        s_m2 = sem("s_m2")
        s_h2 = sem("s_h2")
        s_var = sem("s_var")
        s_sd = sem("s_sd")
        s_scale = sem("s_scale")
        s_bn = sem("s_bn")
        s_u = sem("s_u")
        s_mean = sem("s_mean")
        s_cent = sem("s_cent")
        s_sq = sem("s_sq")
        s_msq = sem("s_msq")
        s_lsd = sem("s_lsd")
        s_ln = sem("s_ln")
        s_tile = sem("s_tile")
        s_ymm = sem("s_ymm")
        s_ya = sem("s_ya")
        s_yd = sem("s_yd")
        s_st = [[sem(f"s_st{a}{b}") for b in range(2)] for a in range(2)]
        s_tbc = [sem(f"s_tbc{h}") for h in range(2)]
        s_toh = sem("s_toh")
        s_oh = sem("s_oh")
        s_inv = sem("s_inv")
        s_wmm = sem("s_wmm")
        s_wgt = sem("s_wgt")
        s_zt = sem("s_zt")
        s_oa = sem("s_oa")
        s_od = sem("s_od")
        s_out = sem("s_out")
        s_dve = sem("s_dve")
        s_dsort = sem("s_dsort")

        PE, DVE = mybir.EngineType.PE, mybir.EngineType.DVE

        def slot_columns(nc, engine, s0):
            return nc.values_load_multi_w_load_instructions(
                offs[0:1, ds(s0, GROUP)], engines=[engine], min_val=0, max_val=NPAD - P,
                skip_runtime_bounds_check_because="offs holds min(block, BLOCKS - 1) * P")[1]

        block = ctx.enter_context(nc.Block())

        @block.sync
        def _(sp):
            for a in range(2):
                for b in range(2):
                    sp.sem_inc(s_st[a][b], 16)
            sp.wait_ge(s_dst0, 1)
            sp.dma_start(dst_i[0:EP, :], dst[0:EFULL].rearrange("(p e) -> p e", e=ECOLS)).then_inc(s_dst, 16)
            sp.dma_start(dst_i[EP:EP + 1, 0:EREST], dst[EFULL:E].rearrange("(p e) -> p e", p=1)).then_inc(s_dst, 16)
            sp.dma_start(dst_next[0:EP, :], dst[1:EFULL + 1].rearrange("(p e) -> p e", e=ECOLS)).then_inc(s_dst, 16)
            sp.dma_start(dst_next[EP:EP + 1, 0:EREST - 1],
                         dst[EFULL + 1:E].rearrange("(p e) -> p e", p=1)).then_inc(s_dst, 16)
            for k, arr in enumerate((src, dst, edge_type)):
                sp.dma_start(edges3[0:CHUNKS - 1, k, :],
                             arr[0:(CHUNKS - 1) * P].rearrange("(c e) -> c e", e=P)).then_inc(s_edges, 16)
                sp.dma_start(edges3[CHUNKS - 1:CHUNKS, k, 0:CREST],
                             arr[(CHUNKS - 1) * P:E].rearrange("(c e) -> c e", c=1)).then_inc(s_edges, 16)
            sp.wait_ge(s_pad, 2)
            sp.dma_start(edges3[CHUNKS - 1:CHUNKS, :, CREST:P], pad_edges[:, :, :]).then_inc(s_edges, 16)
            sp.dma_start(x_in[:, 0:BLOCKS - 1, :],
                         x[0:(BLOCKS - 1) * P, :].rearrange("(t p) f -> p t f", p=P)).then_inc(s_x, 16)
            sp.dma_start(x_in[0:TAIL, BLOCKS - 1, :], x[(BLOCKS - 1) * P:N, :]).then_inc(s_x, 16)

            sp.wait_ge(s_trows, SCOLS)
            sp.dma_start(slot_types[0:(SCOLS - 1) * P, :].rearrange("(j p) e -> p j e", p=P),
                         type_rows[:, 0:SCOLS - 1, :]).then_inc(s_tdram, 16)
            sp.dma_start(slot_types[(SCOLS - 1) * P:SLOTS, :],
                         type_rows[0:SLAST, SCOLS - 1, :]).then_inc(s_tdram, 16)

            def store_tile(t, row, tt, n):
                for hf in range(2):
                    sp.wait_ge(s_ya, t * HPAIR + (3 if hf == 0 else 5) + 2)
                    sp.nop(nofuse=True)
                    sp.wait_ge(s_yd, t * HPAIR + (2 if hf == 0 else 5) + 2)
                    sp.nop(nofuse=True)
                    sp.dma_start(table[ds(row, n), hf * YHALF:(hf + 1) * YHALF],
                                 stage[0:n, tt, hf * YHALF:(hf + 1) * YHALF]).then_inc(s_st[tt][hf], 16)

            with sp.Fori(0, YLOOPS) as it:
                for tt in range(2):
                    store_tile(it * 2 + tt, it * 2 * P + tt * P, tt, P)
            store_tile(BLOCKS - 1, (BLOCKS - 1) * P, 0, TAIL)

            types_flat = slot_types.rearrange("s e -> (s e)")

            def load_types(it, h):
                sp.dma_start(type_bc[:, h, :],
                             types_flat[ds(it * (RING * P) + h * (HALF * P), HALF * P)].partition_broadcast(R)
                             ).then_inc(s_tbc[h], 16)

            sp.wait_ge(s_tdram, 32)
            for h in range(2):
                load_types(0, h)
            with sp.Fori(1, ITERS) as it:
                for h in range(2):
                    sp.wait_ge(s_toh, it * GROUPS + (h + 1) * (GROUPS // 2) - GROUPS)
                    sp.nop(nofuse=True)
                    load_types(it, h)

            for c, (n0, w) in enumerate(CW):
                sp.wait_ge(s_oa if c % 2 == 0 else s_od, c // 2 + 1)
                if w == BANK:
                    sp.dma_start(out[n0:n0 + w, :].rearrange("(t p) f -> p t f", p=P),
                                 y_out[:, c * TPB:(c + 1) * TPB, :]).then_inc(s_out, 16)
                else:
                    sp.dma_start(out[n0:N, :], y_out[0:w, c * TPB, :]).then_inc(s_out, 16)
            sp.wait_ge(s_out, 16 * NBANKS)
            for a in range(2):
                for b in range(2):
                    stores = YLOOPS + (1 if a == 0 else 0)
                    sp.wait_ge(s_st[a][b], 16 + 16 * stores)

        @block.gpsimd
        def _(pool):
            nc.gpsimd.iota(iota_i[:, :], [[1, P]], base=0, channel_multiplier=0)
            nc.gpsimd.iota(part_i[:, :], [[P, SCOLS]], base=0, channel_multiplier=1).then_inc(s_iota, 1)
            nc.gpsimd.memset(pad_edges[:, :, :], 0).then_inc(s_pad, 1)
            pool.wait_ge(s_pad, 1)
            nc.gpsimd.memset(pad_edges[:, 1, :], PAD_DST).then_inc(s_pad, 1)

            pool.wait_ge(s_flag, 1)
            unordered = pool.value_load(flag[0:1, 0:1], min_val=0, max_val=E)
            pool.wait_ge(s_edges, 16 * 7)
            with pool.If(unordered > 0):
                nc.gpsimd.memset(edge_data[:, 0, :], 0)
                nc.gpsimd.memset(edge_data[:, 2, :], 0).then_inc(s_sdata0, 1)
                pool.wait_ge(s_sdata0, 1)
                for k, arr in ((0, src), (2, edge_type)):
                    pool.dma_start(edge_data[0:EP, k, :],
                                   arr[0:EFULL].rearrange("(p e) -> p e", e=ECOLS)).then_inc(s_sdata, 16)
                    pool.dma_start(edge_data[EP:EP + 1, k, 0:EREST],
                                   arr[EFULL:E].rearrange("(p e) -> p e", p=1)).then_inc(s_sdata, 16)
                pool.wait_ge(s_sdata, 64)
                pool.wait_ge(s_pos, 1)

                with pool.Fori(0, ECOLS) as q:
                    nc.gpsimd.tensor_copy(scat_idx[:, :], addr_i[:, :, ds(q, 1)].rearrange("p k e -> p (k e)"))
                    nc.gpsimd.tensor_copy(scat_val[:, :],
                                          edge_data[:, :, ds(q, 1)].rearrange("p k e -> p (k e)")).then_inc(s_scopy, 1)
                    pool.wait_ge(s_scopy, q + 1)
                    pool.nop(nofuse=True)
                    for k in range(3):
                        pool.indirect_dma_start(
                            edges_flat[:, :], bass.IndirectOffsetOnAxis(ap=scat_idx[:, k:k + 1], axis=0),
                            scat_val[:, k:k + 1], None).then_inc(s_scat, 16)
                    pool.wait_ge(s_scat, q * 48 + 48)
                    pool.nop(nofuse=True)

            pool.wait_ge(s_chunk, 1)
            for j in range(SCOLS):
                n = P if j < SCOLS - 1 else SLAST
                pool.indirect_dma_start(slot_rows[0:n, j, :, :].rearrange("p k e -> p (k e)"), None, edges[:, :],
                                        bass.IndirectOffsetOnAxis(ap=slot_chunk_i[0:n, j:j + 1], axis=0)
                                        ).then_inc(s_srows, 16)

            def gather_layer(layer, source, index):
                with pool.Fori(0, ITERS) as it:
                    for h in range(2):
                        pool.wait_ge(s_slot, it * RING + (h + 1) * HALF + layer * SLOTS)
                        nc.gpsimd.tensor_copy(idx_now[:, h * HALF:(h + 1) * HALF],
                                              index[:, ds(it * RING + h * HALF, HALF)]).then_inc(s_idx, 1)
                        pool.wait_ge(s_idx, it * 2 + h + 1 + layer * 2 * ITERS)
                        pool.nop(nofuse=True)
                        for j in range(h * HALF, (h + 1) * HALF):
                            pool.indirect_dma_start(rows[:, j, :], None, source,
                                                    bass.IndirectOffsetOnAxis(ap=idx_now[:, j:j + 1], axis=0)
                                                    ).then_inc(s_row[j], 16)

            pool.wait_ge(s_tables, 4)
            gather_layer(0, x[:, :], src_t)
            for a in range(2):
                for b in range(2):
                    stores = YLOOPS + (1 if a == 0 else 0)
                    pool.wait_ge(s_st[a][b], 16 + 16 * stores)
            gather_layer(1, table_rows, key_t)

        @block.scalar
        def _(act):
            for n, vsrc in enumerate((b1, b2, gamma0, beta0, bias, b_res, gamma1, beta1)):
                act.dma_start(vec[:, n:n + 1], vsrc.rearrange("(p o) -> p o", o=1)).then_inc(s_w, 16)
            for tile, wsrc in ((w1_sb, w1), (w2_sb, w2), (wroot_sb, w_root), (wres_sb, w_res)):
                act.dma_start(tile[:, :], wsrc[:, :]).then_inc(s_w, 16)
            act.dma_start(wrel_sb[:, :, :], w_rel.rearrange("r i o -> i r o")).then_inc(s_wrel, 16)

            for c in range(NBANKS):
                w = min(BANK, NPAD - c * BANK)
                act.wait_ge(s_xtp, c + 1)
                nc.scalar.copy(xT[:, c * BANK:c * BANK + w], bank(c, w)).then_inc(s_xt, 1)

            act.wait_ge(s_w, 16 * 12)
            act.wait_ge(s_const, 1)
            act.wait_ge(s_slot, RING + SLOTS)
            for c, (n0, w) in enumerate(CW):
                nc.scalar.copy(hT[:, n0:n0 + w], bank(c, w)).then_inc(s_h, 1)
            for c, (n0, w) in enumerate(CW):
                act.wait_ge(s_m1, c + 1)
                nc.scalar.activation(gT[:, n0:n0 + w], bank(c, w), ACT.Relu,
                                     bias=vec[:, V_B1:V_B1 + 1]).then_inc(s_h1, 1)
            for c, (n0, w) in enumerate(CW):
                act.wait_ge(s_m2, c + 1)
                nc.scalar.activation(hT[:, n0:n0 + w], bank(c, w), ACT.Relu,
                                     bias=vec[:, V_B2:V_B2 + 1]).then_inc(s_h2, 1)

            def normalise(layer, func):
                act.wait_ge(s_var, layer + 1)
                nc.scalar.activation(bn_sd[:, :], bn2[:, 1:2], ACT.Sqrt, bias=eps_sb[:, :]).then_inc(s_sd, 1)
                act.wait_ge(s_scale, layer + 1)
                for c, (n0, w) in enumerate(CW):
                    nc.scalar.activation(hT[:, n0:n0 + w], hT[:, n0:n0 + w], func,
                                         bias=bn_shift[:, :], scale=bn_scale[:, :]).then_inc(s_bn, 1)
                for c, (n0, w) in enumerate(CW):
                    act.wait_ge(s_cent, layer * NBANKS + c + 1)
                    nc.scalar.activation(sqT[:, n0:n0 + w], hT[:, n0:n0 + w], ACT.Square).then_inc(s_sq, 1)
                for c, (n0, w) in enumerate(CW):
                    act.wait_ge(s_msq, layer * NBANKS + c + 1)
                    nc.scalar.activation(sqT[:, n0:n0 + w], bank(c, w), ACT.Sqrt,
                                         bias=eps_sb[:, :]).then_inc(s_lsd, 1)

            normalise(0, ACT.Identity)

            act.wait_ge(s_ln, NBANKS)
            nc.scalar.copy(x1_tile[:, 0, :], x1T[:, 0:P]).then_inc(s_tile, 1)

            def empty_tile(t, it, tt, n, more):
                for q in range(0, YPAIRS, 2):
                    act.wait_ge(s_ymm, t * YPAIRS + q + 1)
                    if q in (0, 6):
                        act.wait_ge(s_st[tt][q // HPAIR], it * 16 + 16)
                    nc.scalar.copy(stage[0:n, tt, q * 2 * YW:(q + 1) * 2 * YW].rearrange("p (b c) -> p b c", b=2),
                                   bank_pair((tt * YPAIRS + q) % BPAIRS)[0:n]).then_inc(s_ya, 1)
                    if q == 0 and more:
                        nc.scalar.copy(x1_tile[:, 1 - tt, :], x1T[:, ds((t + 1) * P, P)]).then_inc(s_tile, 1)

            with act.Fori(0, YLOOPS) as it:
                for tt in range(2):
                    empty_tile(it * 2 + tt, it, tt, P, True)
            empty_tile(BLOCKS - 1, YLOOPS, 0, TAIL, False)

            act.wait_ge(s_slot, RING + 2 * SLOTS)
            for c, (n0, w) in enumerate(CW):
                nc.scalar.activation(hT[:, n0:n0 + w], bank(c, w), ACT.Identity,
                                     bias=bias_sum[:, :]).then_inc(s_h2, 1)
            normalise(1, ACT.Relu)

            for c in range(0, NBANKS, 2):
                act.wait_ge(s_zt, c + 1)
                w = CW[c][1]
                if w == BANK:
                    nc.scalar.copy(y_out[:, c * TPB:(c + 1) * TPB, :],
                                   bank(c).rearrange("p (t f) -> p t f", f=P)).then_inc(s_oa, 1)
                else:
                    nc.scalar.copy(y_out[0:w, c * TPB, :], bank(c)[0:w, 0:P]).then_inc(s_oa, 1)

        @block.vector
        def _(dve):
            chain = [0]

            def link(ins):
                chain[0] += 1
                ins.then_inc(s_dve, 1)
                dve.wait_ge(s_dve, chain[0])

            nc.vector.memset(dst_i, PAD_DST)
            nc.vector.memset(dst_next, PAD_DST).then_inc(s_dst0, 1)
            nc.vector.memset(ones[:, :], 1.0)
            nc.vector.memset(avg[:, :], 1.0 / D)
            nc.vector.memset(eps_sb[:, :], EPS)
            nc.vector.memset(zeros[:, :], 0.0)
            nc.vector.memset(x1T[:, N:NPAD], 0.0)
            nc.vector.memset(rel_count[:, :], 0.0).then_inc(s_cadd, 1)
            dve.wait_ge(s_iota, 1)
            link(nc.vector.tensor_copy(iota_row[:, :], iota_i[:, :]))
            link(nc.vector.tensor_copy(slot_no[:, :], part_i[:, :]))
            nc.vector.tensor_scalar(before[:, :], iota_row[:, :], slot_no[:, 0:1], None, ALU.is_gt)
            nc.vector.tensor_scalar(ident[:, :], iota_row[:, :], slot_no[:, 0:1], None,
                                    ALU.is_equal).then_inc(s_const, 1)

            dve.wait_ge(s_dst, 64)
            link(nc.vector.tensor_scalar(block_i, dst_i, P.bit_length() - 1, None, ALU.arith_shift_right))
            link(nc.vector.tensor_copy(block_f, block_i))
            link(nc.vector.tensor_tensor(mask, dst_next, dst_i, ALU.is_lt))
            nc.vector.tensor_reduce(counts[:, BUCKETS:BUCKETS + 1], mask, AX.X, ALU.add)
            for b in range(BUCKETS):
                link(nc.vector.tensor_scalar(lane, block_f, float(b), 0.0, ALU.is_equal, ALU.add,
                                             accum_out=counts[:, b:b + 1]))
            dve.sem_inc(s_cnt, 1)

            dve.wait_ge(s_tot, 1)
            link(nc.vector.tensor_copy(tot[:, :], aux[:, 0:BUCKETS + 1]))
            nc.vector.tensor_copy(flag[0:1, 0:1], tot[0:1, BUCKETS:BUCKETS + 1]).then_inc(s_flag, 1)
            link(nc.vector.tensor_tensor_scan(ends[:, :], zeros[:, :], tot[:, 0:BUCKETS], 0.0, ALU.add, ALU.add))
            link(nc.vector.tensor_tensor(starts[:, :], ends[:, :], tot[:, 0:BUCKETS], ALU.subtract))

            link(nc.vector.tensor_tensor(bucket_off[:, :], starts[:, :], aux[:, P:P + BUCKETS], ALU.add))
            link(nc.vector.tensor_scalar(ends_i[:, :], ends[:, :], float(P - 1), None, ALU.add))
            link(nc.vector.tensor_copy(starts_i[:, :], starts[:, :]))
            link(nc.vector.tensor_scalar(ends_i[:, :], ends_i[:, :], P.bit_length() - 1, None, ALU.arith_shift_right))
            link(nc.vector.tensor_scalar(starts_i[:, :], starts_i[:, :], P.bit_length() - 1, None,
                                         ALU.arith_shift_right))
            link(nc.vector.tensor_tensor(span[:, :], ends_i[:, :], starts_i[:, :], ALU.subtract))
            link(nc.vector.memset(nslots[:, :], 0.0))
            link(nc.vector.scalar_tensor_tensor(nslots[:, 0:BLOCKS], tot[:, 0:BLOCKS], 0.0, span[:, 0:BLOCKS],
                                                ALU.is_gt, ALU.mult))
            link(nc.vector.tensor_tensor_scan(slot_end[:, :], zeros[:, :], nslots[:, :], 0.0, ALU.add, ALU.add))
            link(nc.vector.tensor_tensor(shift[:, :], nslots[:, :], slot_end[:, :], ALU.subtract))
            link(nc.vector.tensor_tensor(shift[:, :], shift[:, :], starts_i[:, :], ALU.add))
            for j in range(SCOLS):
                last = nc.vector.tensor_scalar(cmp[:, j, :], slot_end[:, :], slot_no[:, j:j + 1], 0.0,
                                               ALU.is_le, ALU.add, accum_out=slot_block[:, j:j + 1])
            link(last)
            for j in range(SCOLS):
                last = nc.vector.scalar_tensor_tensor(pick[:, j, :], iota_row[:, 0:BUCKETS], slot_block[:, j:j + 1],
                                                      shift[:, :], ALU.is_equal, ALU.mult,
                                                      accum_out=slot_shift[:, j:j + 1])
            link(last)
            link(nc.vector.tensor_tensor(slot_chunk[:, :], slot_no[:, :], slot_shift[:, :], ALU.add))
            nc.vector.tensor_scalar(slot_chunk_i[:, :], slot_chunk[:, :], float(CHUNKS - 1), None,
                                    ALU.min).then_inc(s_chunk, 1)
            link(nc.vector.tensor_scalar(block_base[:, :], slot_block[:, :], float(P), None, ALU.mult))
            nc.vector.tensor_scalar(block_col[:, :], slot_block[:, :], float(BLOCKS - 1), float(P),
                                    ALU.min, ALU.mult).then_inc(s_bcol, 1)

            unordered = dve.value_load(flag[0:1, 0:1], min_val=0, max_val=E)
            with dve.If(unordered > 0):
                nc.vector.memset(zrow, 0.0)
                nc.vector.memset(pos, 0.0).then_inc(s_dsort, 1)
                with dve.Fori(0, BUCKETS) as b:
                    dve.wait_ge(s_dsort, b * 4 + 1)
                    nc.vector.tensor_scalar(mask, block_f, iota_row[:, ds(b, 1)], None,
                                            ALU.is_equal).then_inc(s_dsort, 1)
                    dve.wait_ge(s_dsort, b * 4 + 2)
                    nc.vector.tensor_tensor_scan(rank, zrow, mask, 0.0, ALU.add, ALU.add).then_inc(s_dsort, 1)
                    dve.wait_ge(s_dsort, b * 4 + 3)
                    nc.vector.scalar_tensor_tensor(rank, rank, bucket_off[:, ds(b, 1)], mask,
                                                   ALU.add, ALU.mult).then_inc(s_dsort, 1)
                    dve.wait_ge(s_dsort, b * 4 + 4)
                    nc.vector.tensor_tensor(pos, pos, rank, ALU.add).then_inc(s_dsort, 1)
                done = BUCKETS * 4 + 1
                dve.wait_ge(s_dsort, done)
                nc.vector.tensor_scalar(pos, pos, -1.0, None, ALU.add).then_inc(s_dsort, 1)
                dve.wait_ge(s_dsort, done + 1)
                nc.vector.tensor_copy(pos_i, pos).then_inc(s_dsort, 1)
                dve.wait_ge(s_dsort, done + 2)
                nc.vector.tensor_scalar(hi_i, pos_i, P.bit_length() - 1, None,
                                        ALU.arith_shift_right).then_inc(s_dsort, 1)
                dve.wait_ge(s_dsort, done + 3)
                nc.vector.tensor_copy(hi_f, hi_i).then_inc(s_dsort, 1)
                dve.wait_ge(s_dsort, done + 4)
                nc.vector.scalar_tensor_tensor(pos, hi_f, float(2 * P), pos, ALU.mult,
                                               ALU.add).then_inc(s_dsort, 1)
                dve.wait_ge(s_dsort, done + 5)
                for k in range(3):
                    last = nc.vector.tensor_scalar(addr_i[:, k, :], pos, float(k * P), None, ALU.add)
                last.then_inc(s_pos, 1)

            dve.wait_ge(s_offp, 1)
            nc.vector.tensor_copy(offs[0:1, :], aux[0:1, :]).then_inc(s_off, 1)

            dve.wait_ge(s_srows, 16 * SCOLS)
            for j in range(SCOLS):
                n = P if j < SCOLS - 1 else SLAST
                r = slot_rows[0:n, j]
                v = slot_vals[0:n]
                nc.vector.tensor_copy(v[:, K_SRC, j], r[:, 0])
                nc.vector.tensor_scalar(v[:, K_DLOC, j], r[:, 1], block_base[0:n, j:j + 1], None, ALU.subtract)
                nc.vector.tensor_copy(v[:, K_TYPE, j], r[:, 2])
                nc.vector.scalar_tensor_tensor(v[:, K_KEY, j], r[:, 0], float(R), r[:, 2], ALU.mult,
                                               ALU.add).then_inc(s_vals, 1)
                nc.vector.tensor_copy(type_rows[0:n, j], r[:, 2]).then_inc(s_trows, 1)
            nc.vector.memset(dloc_t[:, SLOTS:], -1.0)
            nc.vector.memset(type_t[:, SLOTS:], -1.0)
            for k, (tab) in enumerate((src_t, dloc_t, type_t, key_t)):
                dve.wait_ge(s_valt, k + 1)
                nc.vector.tensor_copy(tab[:, 0:SLOTS], bank(k, SLOTS)).then_inc(s_tables, 1)
            dve.wait_ge(s_tables, 4)

            def node_onehot(s0, par):
                return nc.vector.tensor_tensor(
                    onehot[:, par], iota_row[:, :].unsqueeze(1).to_broadcast([P, GROUP, P]),
                    dloc_t[:, ds(s0, GROUP)].unsqueeze(2).to_broadcast([P, GROUP, P]), ALU.is_equal)

            def slot_onehots(s0, par):
                node_onehot(s0, par)
                nc.vector.tensor_tensor(
                    onetype[:, par], iota_row[:, 0:R].unsqueeze(1).to_broadcast([P, GROUP, R]),
                    type_t[:, ds(s0, GROUP)].unsqueeze(2).to_broadcast([P, GROUP, R]),
                    ALU.is_equal).then_inc(s_onehot, 1)

            slot_onehots(0, 0)
            with dve.Fori(0, ITERS) as it:
                for g in range(GROUPS):
                    grp = it * GROUPS + g
                    s0 = it * RING + g * GROUP
                    cols = slot_columns(nc, DVE, s0)
                    dve.wait_ge(s_slot, grp * GROUP + RING)
                    slot_onehots(s0 + GROUP, 1 - g % 2)
                    dve.wait_ge(s_cmm, grp + 1)
                    for j in range(GROUP):
                        dve.wait_ge(s_cadd, grp * GROUP + j + 1)
                        dest = rel_count[:, ds(cols[j], P)]
                        nc.vector.tensor_tensor(dest, dest, aux[0:R, j * P:(j + 1) * P],
                                                ALU.add).then_inc(s_cadd, 1)

            def normalise(layer, gam, bet, resid, dest):
                for c, (n0, w) in enumerate(CW):
                    dve.wait_ge(s_h2, layer * NBANKS + c + 1)
                    last = nc.vector.bn_stats(bn6[:, c, :], hT[:, n0:n0 + w])
                link(last)
                link(nc.vector.bn_aggr(bn2[:, :], bn6[:, :, :].rearrange("p c s -> p (c s)")))
                dve.sem_inc(s_var, 1)
                dve.wait_ge(s_sd, layer + 1)
                link(nc.vector.reciprocal(bn_rs[:, :], bn_sd[:, :]))
                link(nc.vector.tensor_tensor(bn_scale[:, :], bn_rs[:, :], vec[:, gam:gam + 1], ALU.mult))
                link(nc.vector.tensor_tensor(bn_ms[:, :], bn2[:, 0:1], bn_scale[:, :], ALU.mult))
                nc.vector.tensor_tensor(bn_shift[:, :], vec[:, bet:bet + 1], bn_ms[:, :],
                                        ALU.subtract).then_inc(s_scale, 1)
                for c, (n0, w) in enumerate(CW):
                    dve.wait_ge(s_bn, layer * NBANKS + c + 1)
                    nc.vector.tensor_tensor(hT[:, n0:n0 + w], hT[:, n0:n0 + w], resid[:, n0:n0 + w],
                                            ALU.add).then_inc(s_u, 1)
                for c, (n0, w) in enumerate(CW):
                    dve.wait_ge(s_mean, layer * NBANKS + c + 1)
                    nc.vector.tensor_tensor(hT[:, n0:n0 + w], hT[:, n0:n0 + w], bank(c, w),
                                            ALU.subtract).then_inc(s_cent, 1)
                for c, (n0, w) in enumerate(CW):
                    dve.wait_ge(s_lsd, layer * NBANKS + c + 1)
                    link(nc.vector.reciprocal(sqT[:, n0:n0 + w], sqT[:, n0:n0 + w]))
                    nc.vector.tensor_tensor(dest[:, n0:n0 + w], hT[:, n0:n0 + w], sqT[:, n0:n0 + w],
                                            ALU.mult).then_inc(s_ln, 1)

            normalise(0, V_G0, V_E0, xT, x1T)
            nc.vector.tensor_tensor(bias_sum[:, :], vec[:, V_BIAS:V_BIAS + 1], vec[:, V_BRES:V_BRES + 1], ALU.add)
            link(nc.vector.tensor_scalar(rel_count[:, :], rel_count[:, :], 1.0, None, ALU.max))
            nc.vector.reciprocal(rel_count[:, :], rel_count[:, :]).then_inc(s_wgt, 1)

            def empty_tile(t, it, tt, n):
                for q in range(1, YPAIRS, 2):
                    dve.wait_ge(s_ymm, t * YPAIRS + q + 1)
                    if q in (1, 5):
                        dve.wait_ge(s_st[tt][q // HPAIR], it * 16 + 16)
                    nc.vector.tensor_copy(
                        stage[0:n, tt, q * 2 * YW:(q + 1) * 2 * YW].rearrange("p (b c) -> p b c", b=2),
                        bank_pair((tt * YPAIRS + q) % BPAIRS)[0:n]).then_inc(s_yd, 1)

            dve.sem_inc(s_yd, 2)
            dve.sem_inc(s_ya, 2)
            with dve.Fori(0, YLOOPS) as it:
                for tt in range(2):
                    empty_tile(it * 2 + tt, it, tt, P)
            empty_tile(BLOCKS - 1, YLOOPS, 0, TAIL)

            with dve.Fori(0, ITERS) as it:
                for g in range(GROUPS):
                    grp = it * GROUPS + g
                    par = g % 2
                    h, gh = divmod(g, GROUPS // 2)
                    if gh == 0:
                        dve.wait_ge(s_tbc[h], it * 16 + 16)
                    nc.vector.tensor_scalar(type_oh[:, par, :], type_bc[:, h, gh * GROUP * P:(gh + 1) * GROUP * P],
                                            slot_no[0:R, 0:1], None, ALU.is_equal).then_inc(s_toh, 1)
                    dve.wait_ge(s_slot, grp * GROUP + RING - GROUP + SLOTS)
                    node_onehot(it * RING + g * GROUP, par).then_inc(s_oh, 1)
                    dve.wait_ge(s_oh, grp + 1)
                    dve.wait_ge(s_wmm, grp + 1)
                    nc.vector.tensor_tensor(onehot[:, par], onehot[:, par],
                                            aux.rearrange("p (g n) -> p g n", g=GROUP), ALU.mult).then_inc(s_wgt, 1)

            dve.sem_inc(s_toh, 1)
            normalise(1, V_G1, V_E1, x1T, gT)
            for c in range(1, NBANKS, 2):
                dve.wait_ge(s_zt, c + 1)
                nc.vector.tensor_copy(y_out[:, c * TPB:(c + 1) * TPB, :],
                                      bank(c).rearrange("p (t f) -> p t f", f=P)).then_inc(s_od, 1)

        @block.tensor
        def _(pe):
            pe.wait_ge(s_const, 1)
            pe.wait_ge(s_cnt, 1)
            nc.tensor.matmul(aux[:, 0:BUCKETS + 1], ones[:, :], counts[:, :], start=True, stop=True)
            nc.tensor.matmul(aux[:, P:P + BUCKETS], before[:, :], counts[:, 0:BUCKETS],
                             start=True, stop=True).then_inc(s_tot, 1)
            pe.wait_ge(s_bcol, 1)
            for j in range(SCOLS):
                last = nc.tensor.matmul(aux[0:1, j * P:(j + 1) * P], block_col[:, j:j + 1], ident[:, :],
                                        start=True, stop=True)
            last.then_inc(s_offp, 1)
            pe.wait_ge(s_vals, SCOLS)
            for k in range(4):
                for j in range(SCOLS):
                    n = P if j < SCOLS - 1 else SLAST
                    last = nc.tensor.transpose(bank(k)[:, j * P:j * P + n], slot_vals[0:n, k, j, :], ident[0:n, 0:n])
                last.then_inc(s_valt, 1)
            pe.wait_ge(s_x, 32)
            pe.wait_ge(s_tables, 4)
            for t in range(BLOCKS):
                n = P if t < BLOCKS - 1 else TAIL
                last = nc.tensor.matmul(acc[:, t * P:(t + 1) * P], x_in[0:n, t, :], ident[0:n, :],
                                        start=(t % TPB == 0), stop=False, skip_group_check=True)
                if t % TPB == TPB - 1 or t == BLOCKS - 1:
                    last.then_inc(s_xtp, 1)
            pe.wait_ge(s_xt, NBANKS)
            pe.sem_inc(s_slot, RING)
            pe.wait_ge(s_off, 1)

            with pe.Fori(0, ITERS) as it:
                for g in range(GROUPS):
                    grp = it * GROUPS + g
                    par = g % 2
                    s0 = it * RING + g * GROUP
                    cols = slot_columns(nc, PE, s0)
                    pe.wait_ge(s_onehot, grp + 1)
                    pe.wait_ge(s_cadd, grp * GROUP + 1)
                    for j in range(GROUP):
                        last = nc.tensor.matmul(aux[0:R, j * P:(j + 1) * P], onetype[:, par, j, :],
                                                onehot[:, par, j, :], start=True, stop=True, skip_group_check=True)
                    last.then_inc(s_cmm, 1)
                    for j in range(GROUP):
                        pe.wait_ge(s_row[g * GROUP + j], it * 16 + 16)
                        nc.tensor.matmul(acc[:, ds(cols[j], P)], rows[:, g * GROUP + j, :], onehot[:, par, j, :],
                                         start=False, stop=False, skip_group_check=True).then_inc(s_slot, 1)

            pe.wait_ge(s_w, 16 * 12)
            for c, (n0, w) in enumerate(CW):
                pe.wait_ge(s_h, c + 1)
                nc.tensor.matmul(bank(c, w), w1_sb[:, :], hT[:, n0:n0 + w], start=True, stop=True).then_inc(s_m1, 1)
            for c, (n0, w) in enumerate(CW):
                pe.wait_ge(s_h1, c + 1)
                nc.tensor.matmul(bank(c, w), w2_sb[:, :], gT[:, n0:n0 + w], start=True, stop=True).then_inc(s_m2, 1)

            def normalise(layer):
                for c, (n0, w) in enumerate(CW):
                    pe.wait_ge(s_u, layer * NBANKS + c + 1)
                    nc.tensor.matmul(bank(c, w), avg[:, :], hT[:, n0:n0 + w],
                                     start=True, stop=True).then_inc(s_mean, 1)
                for c, (n0, w) in enumerate(CW):
                    pe.wait_ge(s_sq, layer * NBANKS + c + 1)
                    nc.tensor.matmul(bank(c, w), avg[:, :], sqT[:, n0:n0 + w],
                                     start=True, stop=True).then_inc(s_msq, 1)

            normalise(0)

            wrel_flat = wrel_sb[:, :, :].rearrange("p r o -> p (r o)")
            pe.wait_ge(s_wrel, 16)

            def table_tile(t, tt, n):
                pe.wait_ge(s_tile, t + 1)
                for q in range(YPAIRS):
                    pe.wait_ge(s_ya if q % 2 == 0 else s_yd, t * HPAIR + q // 2 + 1)
                    dest = bank_pair((tt * YPAIRS + q) % BPAIRS)
                    for b in range(2):
                        col = (2 * q + b) * YW
                        last = nc.tensor.matmul(dest[0:n, b, :], x1_tile[:, tt, 0:n], wrel_flat[:, col:col + YW],
                                                start=True, stop=True)
                    last.then_inc(s_ymm, 1)

            with pe.Fori(0, YLOOPS) as it:
                for tt in range(2):
                    table_tile(it * 2 + tt, tt, P)
            table_tile(BLOCKS - 1, 0, TAIL)

            pe.wait_ge(s_ya, 2 + BLOCKS * HPAIR)
            pe.wait_ge(s_yd, 2 + BLOCKS * HPAIR)
            for c in range(NBANKS):
                w = min(BANK, NPAD - c * BANK)
                nc.tensor.matmul(bank(c, w), wroot_sb[:, :], x1T[:, c * BANK:c * BANK + w],
                                 start=True, stop=False, skip_group_check=True)
                nc.tensor.matmul(bank(c, w), wres_sb[:, :], x1T[:, c * BANK:c * BANK + w],
                                 start=False, stop=False, skip_group_check=True)

            def edge_weights(cols, par):
                for j in range(GROUP):
                    last = nc.tensor.matmul(aux[:, j * P:(j + 1) * P], type_oh[:, par, j * P:(j + 1) * P],
                                            rel_count[:, ds(cols[j], P)], start=True, stop=True,
                                            skip_group_check=True)
                last.then_inc(s_wmm, 1)

            pe.wait_ge(s_toh, 1)
            pe.wait_ge(s_wgt, 1)
            edge_weights(slot_columns(nc, PE, 0), 0)
            with pe.Fori(0, ITERS) as it:
                for g in range(GROUPS):
                    grp = it * GROUPS + g
                    par = g % 2
                    s0 = it * RING + g * GROUP
                    cols = slot_columns(nc, PE, s0)
                    pe.wait_ge(s_wgt, grp + 2)
                    pe.wait_ge(s_toh, grp + 2)
                    edge_weights(slot_columns(nc, PE, s0 + GROUP), 1 - par)
                    for j in range(GROUP):
                        pe.wait_ge(s_row[g * GROUP + j], it * 16 + 16 + 16 * ITERS)
                        nc.tensor.matmul(acc[:, ds(cols[j], P)], rows[:, g * GROUP + j, :], onehot[:, par, j, :],
                                         start=False, stop=False, skip_group_check=True).then_inc(s_slot, 1)

            normalise(1)
            for c, (n0, w) in enumerate(CW):
                pe.wait_ge(s_ln, NBANKS + c + 1)
                for t in range(-(-w // P)):
                    n = min(P, w - t * P)
                    last = nc.tensor.transpose(bank(c)[0:n, t * P:(t + 1) * P],
                                               gT[:, n0 + t * P:n0 + t * P + n], ident[:, :])
                last.then_inc(s_zt, 1)


_INS = ['x', 'src', 'dst', 'edge_type_65', 'L0_gnn_w1', 'L0_gnn_b1', 'L0_gnn_w2', 'L0_gnn_b2', 'L0_gnn_gamma',
        'L0_gnn_beta', 'L1_gnn_W_rel', 'L1_gnn_W_root', 'L1_gnn_bias', 'L1_gnn_W_res', 'L1_gnn_b_res',
        'L1_gnn_gamma', 'L1_gnn_beta']
_OUTS = [((3125, 128), 'float32')]


def kernel(**inputs):
    import numpy as _np
    import concourse.bacc as _bacc
    from concourse import mybir as _mybir
    from concourse.bass_utils import run_bass_kernel_spmd as _run

    nc = _bacc.Bacc("TRN2", target_bir_lowering=False, num_devices=1)
    arrays, args = {}, []
    for name in _INS:
        a = _np.ascontiguousarray(inputs[name])
        arrays[f"in_{name}_dram"] = a
        args.append(nc.dram_tensor(f"in_{name}_dram", a.shape, _mybir.dt.from_np(a.dtype), kind="ExternalInput").ap())
    for i, (shape, dtype) in enumerate(_OUTS):
        dt = _mybir.dt.from_np(_np.dtype(dtype))
        args.append(nc.dram_tensor(f"out_{i}_dram", shape, dt, kind="ExternalOutput").ap())
    gnn_gin_then_relational_kernel(nc, *args)
    r = _run(nc, [arrays], core_ids=[0])
    got = tuple(r.results[0][f"out_{i}_dram"] for i in range(len(_OUTS)))
    return got[0]
```
